# Optimizing a Trainium2 kernel written in Bass

```python
import numpy as np
import jax
import jax.numpy as jnp

def _softmax(x, axis=-1):
    return jax.nn.softmax(x, axis=axis)

def _gelu(x):
    return jax.nn.gelu(x, approximate=True)

def _silu(x):
    return jax.nn.silu(x)

def _sigmoid(x):
    return jax.nn.sigmoid(x)

def _layernorm(x, axis=-1, eps=1e-05):
    m = jnp.mean(x, axis=axis, keepdims=True)
    v = jnp.var(x, axis=axis, keepdims=True)
    return (x - m) / jnp.sqrt(v + eps)

def _scatter_add(tgt, idx, src, axis=0):
    return tgt.at[idx].add(src)

def _segment_sum(src, seg, n):
    return jax.ops.segment_sum(src, seg, n)
kernel_name = 'mk_cond_resid_d2_seqx_r4_fbd8c3'

def setup_inputs(seed: int=0):
    np.random.seed(seed)
    _w = jnp.asarray

    def _rec_inputs():
        import jax
        import jax.numpy as jnp
        _rk = jax.random.key(seed)
        x = 7.22e-05 + 1 * jax.random.normal(jax.random.fold_in(_rk, 1), (8, 256, 1024), jnp.float32)
        _lenS = 256 - jax.random.randint(jax.random.fold_in(_rk, 7), (8,), 0, max(1, 256 // 4) + 1, jnp.int32)
        _lenS2 = 256 - jax.random.randint(jax.random.fold_in(_rk, 8), (8,), 0, max(1, 256 // 4) + 1, jnp.int32)
        condB_coeff = 0.00219231 + 0.0100837 * jax.random.normal(jax.random.fold_in(_rk, 11), (8,), jnp.float32)
        itok_B_3_7 = jax.random.randint(jax.random.fold_in(_rk, 13), (8,), 3, 8, jnp.int32)
        _validS = jnp.arange(256)[None, :] < _lenS[:, None]
        _validS2 = jnp.arange(256)[None, :] < _lenS2[:, None]
        _causal = jnp.tril(jnp.ones((256, 256), dtype=bool))
        mask_Bx4096x4096_ik1 = jnp.where(jnp.ones((8, 1024, 1024), dtype=bool), 1, 0).astype(jnp.int32)
        return (x, condB_coeff, itok_B_3_7, mask_Bx4096x4096_ik1)
    x, condB_coeff, itok_B_3_7, mask_Bx4096x4096_ik1 = _rec_inputs()

    def _L0_cond_setup():
        import jax, jax.numpy as jnp
        import numpy as np
        B, S, D_IN, D_OUT = (4, 128, 1024, 1024)
        key = jax.random.key(seed)
        k1, k2, k3, k4, k5 = jax.random.split(key, 5)
        hidden_states = jax.random.normal(k1, (B, S, D_IN), dtype=jnp.float32)
        W = jax.random.normal(k2, (D_OUT, D_IN), dtype=jnp.float32) * 0.02
        b = jax.random.normal(k3, (D_OUT,), dtype=jnp.float32) * 0.02
        coeff = jax.random.normal(k4, (B,), dtype=jnp.float32) * 0.01
        mask = jax.random.randint(k5, (B, D_IN, D_OUT), 0, 2, dtype=jnp.int32)
        return {'hidden_states': hidden_states, 'W': W, 'b': b, 'coeff': coeff, 'mask': mask}
    _L0_cond_all = _L0_cond_setup()
    _L0_cond_in = {k: v for k, v in _L0_cond_all.items() if k in ('W', 'b')}
    del _L0_cond_all

    def _L1_cond_setup():
        import jax, jax.numpy as jnp
        import numpy as np
        MAX_LORAS, OUT, IN = (8, 1024, 1024)
        B, S = (4, 512)
        key = jax.random.key(seed)
        k1, k2, k3 = jax.random.split(key, 3)
        x = jax.random.normal(k1, (B, S, IN), dtype=jnp.float32)
        weight = jax.random.normal(k2, (MAX_LORAS, OUT, IN), dtype=jnp.float32) * 0.02
        adapter_ids = jax.random.randint(k3, (B,), 0, MAX_LORAS, dtype=jnp.int32)
        return {'x': x, 'weight': weight, 'adapter_ids': adapter_ids}
    _L1_cond_all = _L1_cond_setup()
    _L1_cond_in = {k: v for k, v in _L1_cond_all.items() if k in ('weight',)}
    del _L1_cond_all
    return {'x': x, 'condB_coeff': condB_coeff, 'itok_B_3_7': itok_B_3_7, 'mask_Bx4096x4096_ik1': mask_Bx4096x4096_ik1, 'L0_cond_W': _L0_cond_in['W'], 'L0_cond_b': _L0_cond_in['b'], 'L1_cond_weight': _L1_cond_in['weight']}

def reference(x, condB_coeff, itok_B_3_7, mask_Bx4096x4096_ik1, L0_cond_W, L0_cond_b, L1_cond_weight):
    import jax
    import jax.numpy as jnp

    def _L0_cond_ref(hidden_states, W, b, coeff, mask):
        import jax, jax.numpy as jnp
        import numpy as np
        B, S, D_IN, D_OUT = (4, 128, 1024, 1024)
        output = jnp.einsum('bsi,oi->bso', hidden_states, W) + b
        sign = (2 * mask - 1).astype(hidden_states.dtype)
        diff = jnp.einsum('bsi,bio->bso', hidden_states, sign)
        return output + diff * coeff[:, None, None]

    def _L1_cond_ref(x, weight, adapter_ids):
        import jax, jax.numpy as jnp
        import numpy as np
        MAX_LORAS, OUT, IN = (8, 1024, 1024)
        B, S = (4, 512)
        w = weight[adapter_ids]
        return jnp.einsum('bsi,boi->bso', x, w)
    x = x + _L0_cond_ref(x, L0_cond_W, L0_cond_b, condB_coeff, mask_Bx4096x4096_ik1)
    x = x + _L1_cond_ref(x, L1_cond_weight, itok_B_3_7)
    return x

_drawn_inputs = setup_inputs


def setup_inputs(seed=0):
    import zlib

    import numpy as np

    out = dict(_drawn_inputs(seed))
    spreads = {}
    factors = {'L0_cond_b': 3.624}
    for name, (base, spread) in spreads.items():
        noise = np.random.default_rng([zlib.crc32(name.encode()), seed]).standard_normal(out[name].shape)
        drawn = base * np.exp(spread * noise) if base else spread * noise
        out[name] = jnp.asarray(drawn.astype(out[name].dtype))
    for name, factor in factors.items():
        out[name] = (out[name] * factor).astype(out[name].dtype)
    return out
```

```python
from contextlib import ExitStack

import concourse.bass as bass
from concourse import mybir

P = 128
SQ = 32

F32 = mybir.dt.float32
F32R = mybir.dt.float32r
I32 = mybir.dt.int32
ALU = mybir.AluOpType
ACT = mybir.ActivationFunctionType

M_AHEAD = 3
W_AHEAD = 3
T_AHEAD = 2
DMA = 16


X_PAIRS = {1: (0,), 2: (1,), 4: (2,), 6: (3,)}
X_PAIRS_LEAD = {5: (0, 1), 6: (2, 3)}


def stages(kind, u):
    return {
        "turn_W": kind == "lead" or (kind == "first" and u < 8 - W_AHEAD),
        "turn_w": (kind == "first" and u >= 8 - T_AHEAD) or kind in ("steady", "last")
        or (kind == "drain" and u < 8 - T_AHEAD),
        "form_M": kind in ("lead", "first", "steady") or (kind == "last" and u < 8 - M_AHEAD),
        "sign": kind in ("lead", "first", "steady") or (kind == "last" and u < 8 - M_AHEAD - 1),
        "x_pairs": X_PAIRS_LEAD.get(u, ()) if kind == "lead"
        else X_PAIRS.get(u, ()) if kind in ("first", "steady") else (),
        "first": kind in ("first", "steady", "last"),
        "second": kind in ("steady", "last", "drain"),
    }


def build(nc, x, coeff, ids, mask, W, bias, weight, out):
    B, S, D = x.shape
    K = D // P
    ST = S // P
    CH = S // SQ
    Q = D // 4
    GRP = P // SQ
    assert K == 8 and ST == 2 and CH == K and Q == 2 * P and B >= 4 and B % 2 == 0

    with ExitStack() as ctx:
        def sb(name, shape, dt):
            return ctx.enter_context(nc.sbuf_tensor(name, shape, dt))

        def sem(name):
            return ctx.enter_context(nc.semaphore(name))

        ident = sb("ident", [P, P], F32)
        WT = sb("WT", [P, K, D], F32)
        coeffs = sb("coeffs", [P, B], F32)
        bias_col = sb("bias_col", [P, K], F32)
        ids_row = sb("ids_row", [1, B], I32)
        natural = sb("natural", [P, 4, D], F32)
        masks = sb("masks", [P, 2, K, Q], I32)
        M_hi = sb("M_hi", [P, 4, K, P], F32R)
        M_lo = sb("M_lo", [P, 4, K, P], F32R)
        w_hi = sb("w_hi", [P, 2, K, Q], F32R)
        w_lo = sb("w_lo", [P, 2, K, Q], F32R)
        x_nat = sb("x_nat", [P, CH, Q], F32)
        x_turned = sb("x_turned", [P, K, 2 * SQ], F32)
        x_hi = sb("x_hi", [P, 2, K, S], F32R)
        x_lo = sb("x_lo", [P, 2, K, S], F32R)
        h_hi = sb("h_hi", [P, 2, K, S], F32R)
        h_lo = sb("h_lo", [P, 2, K, S], F32R)
        out_sb = sb("out_sb", [P, 4, Q], F32)
        turn_ps = ctx.enter_context(nc.psum_tensor("turn_ps", [P, 2, K, P], F32))
        first_ps = ctx.enter_context(nc.psum_tensor("first_ps", [P, 2, 512], F32))
        second_ps = ctx.enter_context(nc.psum_tensor("second_ps", [P, 2, 512], F32))

        ids_loaded = sem("ids_loaded")
        consts_loaded = sem("consts_loaded")
        ident_steps = sem("ident_steps")
        natural_loaded = [sem(f"natural_loaded{i}") for i in range(4)]
        mask_loaded = [sem(f"mask_loaded{i}") for i in range(2)]
        x_loaded = sem("x_loaded")
        diag_added = sem("diag_added")
        tile_turned = sem("tile_turned")
        act_took = sem("act_took")
        dve_took = sem("dve_took")
        sign_done = sem("sign_done")
        sum_done = sem("sum_done")
        M_hi_done = sem("M_hi_done")
        M_done = sem("M_done")
        x_turn_done = sem("x_turn_done")
        x_hi_done = sem("x_hi_done")
        x_done = sem("x_done")
        first_done = sem("first_done")
        h_hi_done = sem("h_hi_done")
        h_done = sem("h_done")
        second_done = sem("second_done")
        out_taken = sem("out_taken")
        stored = [sem(f"stored{i}") for i in range(4)]

        bias_dram = bias.rearrange("(k p) -> p k", p=P)
        coeff_dram = coeff.rearrange("(a b) -> a b", a=1).to_broadcast([P, B])

        block = ctx.enter_context(nc.Block())

        def batches(eng, slot):
            for u in range(K - M_AHEAD, K):
                slot("lead", -1, u, 1)
            for u in range(K):
                slot("first", 0, u, 0)
            with eng.Fori(0, (B - 2) // 2) as i:
                for par in (1, 0):
                    b = 2 * i + (1 if par else 2)
                    for u in range(K):
                        slot("steady", b, u, par)
            for u in range(K):
                slot("last", B - 1, u, (B - 1) % 2)
            for u in range(K):
                slot("drain", B, u, B % 2)

        @block.sync
        def _(sp):
            def load_W(t):
                sp.dma_start(natural[:, t % 4, :], W[t * P:(t + 1) * P, :]).then_inc(natural_loaded[t % 4], DMA)

            def load_mask(b, q):
                sp.dma_start(masks[:, q % 2, :, :],
                             mask[bass.ds(b, 1), :, q * Q:(q + 1) * Q].rearrange("a (p k) c -> p (a k) c", k=K)
                             ).then_inc(mask_loaded[q % 2], DMA)

            def load_x(b):
                for a in range(GRP):
                    sp.dma_start(x_nat[a * SQ:(a + 1) * SQ, :, :],
                                 x[bass.ds(b, 1), :, a * Q:(a + 1) * Q].rearrange("a (c r) i -> r (a c) i", r=SQ)
                                 ).then_inc(x_loaded, DMA)

            sp.dma_start(ids_row[:, :], ids.rearrange("(a b) -> a b", a=1)).then_inc(ids_loaded, DMA)
            load_W(0)
            load_mask(0, 0)
            sp.dma_start(coeffs[:, :], coeff_dram).then_inc(consts_loaded, DMA)
            load_x(0)
            load_W(1)
            load_W(2)
            load_mask(0, 1)
            with nc.allow_non_contiguous_dma(reason="4 KiB of bias, once"):
                sp.dma_start(bias_col[:, :], bias_dram).then_inc(consts_loaded, DMA)
            sp.wait_ge(ids_loaded, DMA)

            def slot(kind, b, u, par):
                on = stages(kind, u)
                if kind == "lead" or (kind == "first" and u < 8 - W_AHEAD - 3):
                    t = 8 * b + u + W_AHEAD + 3
                    if t >= 4:
                        sp.wait_ge(tile_turned, t - 3)
                    load_W(t)
                elif (kind == "first" and u >= 5 - T_AHEAD) or kind in ("steady", "last") \
                        or (kind == "drain" and u < 5 - T_AHEAD):
                    m = (u + T_AHEAD + 3) % 8
                    bw = b - 1 + (u + T_AHEAD + 3) // 8
                    who = sp.value_load(ids_row[0:1, bass.ds(bw, 1)], min_val=0, max_val=weight.shape[0] - 1)
                    sp.wait_ge(tile_turned, 8 * bw + m + 5)
                    sp.dma_start(natural[:, m % 4, :],
                                 weight[bass.ds(who, 1), m * P:(m + 1) * P, :].rearrange("a p i -> (a p) i")
                                 ).then_inc(natural_loaded[m % 4], DMA)
                q = (u + 5) // 2
                if u % 2 == 1 and (kind in ("first", "steady") or (kind == "lead" and u == 7)
                                   or (kind == "last" and q < 4)):
                    sp.wait_ge(M_done, 8 * b + u + M_AHEAD)
                    load_mask(b + q // 4, q % 4)
                if u == 0 and kind in ("first", "steady"):
                    sp.wait_ge(x_turn_done, 4 * (b + 1))
                    load_x(b + 1)
                if on["second"]:
                    sp.wait_ge(out_taken, 8 * (b - 1) + u + 3)
                    s, q = u % ST, u // ST
                    sp.dma_start(out[bass.ds(b - 1, 1), s * P:(s + 1) * P, q * Q:(q + 1) * Q]
                                 .rearrange("a p c -> (a p) c"), out_sb[:, u % 4, :]).then_inc(stored[u % 4], DMA)

            batches(sp, slot)
            for i in range(4):
                sp.wait_ge(stored[i], DMA * (B * K // 4 + 1))

        @block.gpsimd
        def _(pool):
            nc.gpsimd.memset(ident[:, :], 0.0).then_inc(ident_steps, 1)
            pool.wait_ge(ident_steps, 1)
            nc.gpsimd.affine_select(out=ident[:, :], in_=ident[:, :], compare_op=ALU.not_equal, fill=1.0, base=0,
                                    pattern=[[-1, P]], channel_multiplier=1).then_inc(ident_steps, 1)
            pool.wait_ge(ident_steps, 2)
            with pool.Fori(0, B + 1) as i:
                for t in range(K):
                    pool.wait_ge(natural_loaded[t % 4], DMA * (2 * i + t // 4 + 1))
                    block_t = natural[:, t % 4, t * P:(t + 1) * P]
                    nc.gpsimd.tensor_tensor(block_t, block_t, ident[:, :], ALU.add).then_inc(diag_added, 1)

        @block.tensor
        def _(pe):
            pe.wait_ge(ident_steps, 2)

            def turn(r, columns):
                for k in range(K):
                    done = nc.tensor.transpose(turn_ps[:, r % 2, k, :], columns(natural[:, r % 4, :], k), ident[:, :])
                done.then_inc(tile_turned, 1)

            def product(acc, terms):
                for k in range(K):
                    for j, (left, right) in enumerate(terms(k)):
                        done = nc.tensor.matmul(acc, left, right, start=(k == 0 and j == 0),
                                                stop=(k == K - 1 and j == 2))
                return done

            def slot(kind, b, u, par):
                on = stages(kind, u)
                if on["turn_W"]:
                    t = 8 * b + u + W_AHEAD
                    pe.wait_ge(diag_added, t + 1)
                    if t >= 2:
                        pe.wait_ge(act_took, t - 1)
                        pe.wait_ge(dve_took, t - 1)
                    turn(t, lambda tile, k: tile[:, k:D:K])
                if on["turn_w"]:
                    m = u + T_AHEAD
                    pe.wait_ge(diag_added, 8 * b + m + 1)
                    pe.wait_ge(act_took, 8 * b + m - 1)
                    pe.wait_ge(dve_took, 8 * b + m - 1)
                    turn(m, lambda tile, k: tile[:, k * P:(k + 1) * P])
                if on["first"]:
                    if u == 0:
                        pe.wait_ge(x_done, 4 * (b + 1))
                    pe.wait_ge(M_done, 8 * b + u + 1)
                    if kind != "first" or u >= 2:
                        pe.wait_ge(h_done, 8 * b + u - 1)
                    product(first_ps[:, u % 2, 0:S], lambda k: (
                        (M_hi[:, u % 4, k, :], x_lo[:, par, k, :]),
                        (M_hi[:, u % 4, k, :], x_hi[:, par, k, :]),
                        (M_lo[:, u % 4, k, :], x_hi[:, par, k, :]))).then_inc(first_done, 1)
                if on["second"]:
                    s, q = u % ST, u // ST
                    if u == 0:
                        pe.wait_ge(h_done, 8 * b)
                    if s == 0:
                        pe.wait_ge(dve_took, 8 * b + u + 2)
                    pe.wait_ge(out_taken, 8 * (b - 1) + u + 1)
                    rows = slice(s * P, (s + 1) * P)
                    product(second_ps[:, u % 2, 0:Q], lambda k: (
                        (h_hi[:, 1 - par, k, rows], w_lo[:, q % 2, k, :]),
                        (h_hi[:, 1 - par, k, rows], w_hi[:, q % 2, k, :]),
                        (h_lo[:, 1 - par, k, rows], w_hi[:, q % 2, k, :]))).then_inc(second_done, 1)

            batches(pe, slot)

        @block.scalar
        def _(act):
            act.sem_inc(out_taken, 2)
            for i in range(4):
                act.sem_inc(stored[i], DMA)
            act.wait_ge(mask_loaded[0], DMA)

            def sign(v):
                at = masks[:, (v // 2) % 2, :, (v % 2) * P:(v % 2 + 1) * P]
                nc.scalar.activation(at.bitcast(F32), at, ACT.Copy, scale=2.0, bias=-1.0).then_inc(sign_done, 1)

            sign(0)

            def slot(kind, b, u, par):
                on = stages(kind, u)
                v = u + M_AHEAD
                if on["turn_W"]:
                    t = 8 * b + u + W_AHEAD
                    act.wait_ge(tile_turned, t + 1)
                    nc.scalar.copy(WT[:, 0:K // 2, t * P:(t + 1) * P], turn_ps[:, t % 2, 0:K // 2, :]
                                   ).then_inc(act_took, 1)
                if on["turn_w"]:
                    m = u + T_AHEAD
                    act.wait_ge(tile_turned, 8 * b + m + 1)
                    nc.scalar.copy(w_hi[:, m // 2 % 2, :, (m % 2) * P:(m % 2 + 1) * P], turn_ps[:, m % 2, :, :]
                                   ).then_inc(act_took, 1)
                if on["form_M"]:
                    act.wait_ge(sum_done, 8 * b + v + 1)
                    nc.scalar.copy(M_hi[:, v % 4, :, :],
                                   masks[:, v // 2 % 2, :, (v % 2) * P:(v % 2 + 1) * P].bitcast(F32)
                                   ).then_inc(M_hi_done, 1)
                for j in on["x_pairs"]:
                    act.wait_ge(x_turn_done, 4 * (b + 1) + j + 1)
                    nc.scalar.copy(x_hi[:, 1 - par, :, j * 2 * SQ:(j + 1) * 2 * SQ], x_turned[:, :, :]
                                   ).then_inc(x_hi_done, 1)
                if on["sign"]:
                    if (v + 1) % 2 == 0:
                        q = (v + 1) // 2
                        act.wait_ge(mask_loaded[q % 2], DMA * (2 * b + q // 2 + 1))
                    sign(v + 1)
                if on["first"]:
                    if kind == "first" and u == 0:
                        act.wait_ge(consts_loaded, 2 * DMA)
                    act.wait_ge(first_done, 8 * b + u + 1)
                    nc.scalar.activation(h_hi[:, par, u, :], first_ps[:, u % 2, 0:S], ACT.Identity,
                                         bias=bias_col[:, u:u + 1], scale=1.0).then_inc(h_hi_done, 1)
                if on["second"]:
                    act.wait_ge(second_done, 8 * (b - 1) + u + 1)
                    act.wait_ge(stored[u % 4], DMA * (2 * b - 1 + u // 4))
                    nc.scalar.copy(out_sb[:, u % 4, :], second_ps[:, u % 2, 0:Q]).then_inc(out_taken, 1)

            batches(act, slot)

        @block.vector
        def _(dve):
            def split_h(b, u, par):
                dve.wait_ge(h_hi_done, 8 * b + u + 1)
                nc.vector.scalar_tensor_tensor(out=h_lo[:, par, u, :], in0=first_ps[:, u % 2, 0:S],
                                               scalar=bias_col[:, u:u + 1], in1=h_hi[:, par, u, :].bitcast(F32),
                                               op0=ALU.add, op1=ALU.subtract).then_inc(h_done, 1)

            def turn_x(b, j):
                dve.wait_ge(x_loaded, GRP * DMA * (b + 2))
                dve.wait_ge(x_done, 4 * (b + 1) + j)
                for c in range(2):
                    done = nc.vector.transpose(
                        x_turned[:, :, c * SQ:(c + 1) * SQ],
                        x_nat[:, 2 * j + c, :].rearrange("p (i k) -> p k i", k=K))
                done.then_inc(x_turn_done, 1)

            def split_x(b, j, par):
                dve.wait_ge(x_hi_done, 4 * (b + 1) + j + 1)
                at = slice(j * 2 * SQ, (j + 1) * 2 * SQ)
                nc.vector.tensor_tensor(x_lo[:, 1 - par, :, at], x_turned[:, :, :], x_hi[:, 1 - par, :, at].bitcast(F32),
                                        ALU.subtract).then_inc(x_done, 1)

            dve.wait_ge(consts_loaded, 2 * DMA)

            def slot(kind, b, u, par):
                on = stages(kind, u)
                v = u + M_AHEAD
                if on["turn_W"]:
                    t = 8 * b + u + W_AHEAD
                    dve.wait_ge(tile_turned, t + 1)
                    nc.vector.tensor_copy(WT[:, K // 2:K, t * P:(t + 1) * P], turn_ps[:, t % 2, K // 2:K, :]
                                          ).then_inc(dve_took, 1)
                    dve.wait_ge(act_took, t + 1)
                    dve.wait_ge(dve_took, t + 1)
                unit = masks[:, v // 2 % 2, :, (v % 2) * P:(v % 2 + 1) * P].bitcast(F32)
                if on["form_M"]:
                    dve.wait_ge(sign_done, 8 * b + v + 1)
                    o = v % 8 * P
                    nc.vector.scalar_tensor_tensor(out=unit, in0=unit, scalar=coeffs[:, bass.ds(b + v // 8, 1)],
                                                   in1=WT[:, :, o:o + P], op0=ALU.mult, op1=ALU.add
                                                   ).then_inc(sum_done, 1)
                if on["x_pairs"] and kind != "lead":
                    turn_x(b, on["x_pairs"][0])
                if on["turn_w"]:
                    m = u + T_AHEAD
                    at = slice((m % 2) * P, (m % 2 + 1) * P)
                    dve.wait_ge(act_took, 8 * b + m + 1)
                    nc.vector.tensor_tensor(w_lo[:, m // 2 % 2, :, at], turn_ps[:, m % 2, :, :],
                                            w_hi[:, m // 2 % 2, :, at].bitcast(F32), ALU.subtract
                                            ).then_inc(dve_took, 1)
                if on["form_M"]:
                    dve.wait_ge(M_hi_done, 8 * b + v + 1)
                    nc.vector.tensor_tensor(M_lo[:, v % 4, :, :], unit, M_hi[:, v % 4, :, :].bitcast(F32), ALU.subtract
                                            ).then_inc(M_done, 1)
                if on["x_pairs"] and kind != "lead":
                    split_x(b, on["x_pairs"][0], par)
                if kind == "lead":
                    for j in on["x_pairs"]:
                        turn_x(b, j)
                        split_x(b, j, par)
                if on["first"]:
                    split_h(b, u, par)

            batches(dve, slot)


_INS = ["x", "condB_coeff", "itok_B_3_7", "mask_Bx4096x4096_ik1", "L0_cond_W", "L0_cond_b", "L1_cond_weight"]
_OUTS = [((8, 256, 1024), "float32")]


def kernel(**inputs):
    import numpy as _np
    import concourse.bacc as _bacc
    from concourse import mybir as _mybir
    from concourse.bass_utils import run_bass_kernel_spmd as _run

    nc = _bacc.Bacc("TRN2", target_bir_lowering=False, num_devices=1)
    arrays, args = {}, []
    for name in _INS:
        a = _np.ascontiguousarray(inputs[name])
        arrays[f"in_{name}_dram"] = a
        args.append(nc.dram_tensor(f"in_{name}_dram", a.shape, _mybir.dt.from_np(a.dtype), kind="ExternalInput").ap())
    for i, (shape, dtype) in enumerate(_OUTS):
        dt = _mybir.dt.from_np(_np.dtype(dtype))
        args.append(nc.dram_tensor(f"out_{i}_dram", shape, dt, kind="ExternalOutput").ap())
    build(nc, *args)
    r = _run(nc, [arrays], core_ids=[0])
    got = tuple(r.results[0][f"out_{i}_dram"] for i in range(len(_OUTS)))
    return got[0]
```

```python
from contextlib import ExitStack

import concourse.bass as bass
from concourse import mybir

P = 128
SQ = 32

F32 = mybir.dt.float32
F32R = mybir.dt.float32r
I32 = mybir.dt.int32
ALU = mybir.AluOpType
ACT = mybir.ActivationFunctionType

M_AHEAD = 1
W_AHEAD = M_AHEAD + 2
T_AHEAD = 2
DVE_UNITS = 6
DMA = 16


X_PAIRS = {3: (0,), 4: (1,), 5: (2,), 6: (3,)}
X_PAIRS_FIRST = {3: (0, 1), 4: (2,), 5: (3,)}


def stages(kind, u):
    return {
        "turn_W": (0, 1) if kind == "lead" and u == 7 - M_AHEAD else (u - 8 + W_AHEAD,) if kind == "lead"
        else (u + W_AHEAD,) if kind == "first" and u < 8 - W_AHEAD else (),
        "turn_w": (kind == "first" and u >= 8 - T_AHEAD) or kind in ("steady", "last")
        or (kind == "drain" and u < 8 - T_AHEAD),
        "split_M": (kind == "lead" and u >= 8 - M_AHEAD) or kind in ("first", "steady")
        or (kind == "last" and u < 8 - M_AHEAD),
        "sum_M": kind in ("lead", "first", "steady") or (kind == "last" and u < 8 - M_AHEAD - 1),
        "x_pairs": (0, 1, 2, 3) if kind == "lead" and u == 7 - M_AHEAD
        else X_PAIRS_FIRST.get(u, ()) if kind == "first" else X_PAIRS.get(u, ()) if kind == "steady" else (),
        "first": kind in ("first", "steady", "last"),
        "second": kind in ("steady", "last", "drain"),
    }


def by_dve(m):
    return m < DVE_UNITS


def adds_diagonal(m):
    return not by_dve(m) or m % 2 == m // 4


def up_to(what, b, m, of=range(8)):
    return sum(what(j) for j in of) * b + sum(what(j) for j in of if j <= m)


def build(nc, x, coeff, ids, mask, W, bias, weight, out):
    B, S, D = x.shape
    K = D // P
    ST = S // P
    CH = S // SQ
    Q = D // 4
    GRP = P // SQ
    HALF = D // 2
    assert K == 8 and ST == 2 and CH == K and Q == 2 * P and B >= 4 and B % 2 == 0

    with ExitStack() as ctx:
        def sb(name, shape, dt):
            return ctx.enter_context(nc.sbuf_tensor(name, shape, dt))

        def sem(name):
            return ctx.enter_context(nc.semaphore(name))

        ident = sb("ident", [P, P], F32)
        WT = sb("WT", [P, K, D], F32)
        coeffs = sb("coeffs", [P, B], F32)
        bias_col = sb("bias_col", [P, K], F32)
        ids_row = sb("ids_row", [1, B], I32)
        natural = sb("natural", [P, 4, D], F32)
        masks = sb("masks", [P, 2, K, HALF], I32)
        M_hi = sb("M_hi", [P, 2, K, P], F32R)
        M_lo = sb("M_lo", [P, 2, K, P], F32R)
        w_hi = sb("w_hi", [P, 2, K, Q], F32R)
        w_lo = sb("w_lo", [P, 2, K, Q], F32R)
        x_nat = sb("x_nat", [P, CH, Q], F32)
        x_turned = sb("x_turned", [P, 2, K, 2 * SQ], F32)
        x_hi = sb("x_hi", [P, 2, K, S], F32R)
        x_lo = sb("x_lo", [P, 2, K, S], F32R)
        h_hi = sb("h_hi", [P, 2, K, S], F32R)
        h_lo = sb("h_lo", [P, 2, K, S], F32R)
        out_sb = sb("out_sb", [P, 2, Q], F32)
        turn_ps = ctx.enter_context(nc.psum_tensor("turn_ps", [P, 2, K, P], F32))
        first_ps = ctx.enter_context(nc.psum_tensor("first_ps", [P, 2, 512], F32))
        second_ps = ctx.enter_context(nc.psum_tensor("second_ps", [P, 2, 512], F32))

        ids_loaded = sem("ids_loaded")
        coeffs_loaded = sem("coeffs_loaded")
        bias_loaded = sem("bias_loaded")
        ident_steps = sem("ident_steps")
        natural_loaded = [sem(f"natural_loaded{i}") for i in range(4)]
        mask_loaded = [sem(f"mask_loaded{i}") for i in range(2)]
        x_loaded = sem("x_loaded")
        diag_added = sem("diag_added")
        half_diag_added = sem("half_diag_added")
        tile_turned = sem("tile_turned")
        unit_turned = sem("unit_turned")
        act_took = sem("act_took")
        dve_took = sem("dve_took")
        sign_done = sem("sign_done")
        sum_done = sem("sum_done")
        M_hi_done = sem("M_hi_done")
        M_done = sem("M_done")
        x_turn_done = sem("x_turn_done")
        x_hi_done = sem("x_hi_done")
        x_done = sem("x_done")
        first_done = sem("first_done")
        h_hi_done = sem("h_hi_done")
        h_done = sem("h_done")
        second_done = sem("second_done")
        out_taken = sem("out_taken")
        stored = [sem(f"stored{i}") for i in range(2)]

        bias_dram = bias.rearrange("(h p k) -> p h k", p=P, k=4)
        coeff_dram = coeff.rearrange("(a b) -> a b", a=1).to_broadcast([P, B])

        def unit(v):
            return masks[:, v // 4 % 2, :, v % 4:HALF:4]

        def out_columns(u):
            return slice(u // 4 * HALF + u % 4, (u // 4 + 1) * HALF, 4)

        def landed(b, m):
            return DMA * (2 + up_to(lambda j: GRP if by_dve(j) else 1, b, m, of=(m % 4, m % 4 + 4)))

        def diagonals(b, m):
            return K + up_to(adds_diagonal, b, m)

        def turned(b, m):
            return up_to(by_dve, b, m) if by_dve(m) else K + up_to(lambda j: not by_dve(j), b, m)

        block = ctx.enter_context(nc.Block())

        def batches(eng, slot):
            for u in range(K - M_AHEAD - 1, K):
                slot("lead", -1, u, 1)
            for u in range(K):
                slot("first", 0, u, 0)
            with eng.Fori(0, (B - 2) // 2) as i:
                for par in (1, 0):
                    b = 2 * i + (1 if par else 2)
                    for u in range(K):
                        slot("steady", b, u, par)
            for u in range(K):
                slot("last", B - 1, u, (B - 1) % 2)
            for u in range(K):
                slot("drain", B, u, B % 2)

        @block.sync
        def _(sp):
            def load_W(t):
                sp.dma_start(natural[:, t % 4, :], W[out_columns(t), :]).then_inc(natural_loaded[t % 4], DMA)

            def load_mask(b, half):
                sp.dma_start(masks[:, half, :, :],
                             mask[bass.ds(b, 1), :, half * HALF:(half + 1) * HALF]
                             .rearrange("a (p k) c -> p (a k) c", k=K)).then_inc(mask_loaded[half], DMA)

            def load_x(b):
                for a in range(GRP):
                    sp.dma_start(x_nat[a * SQ:(a + 1) * SQ, :, :],
                                 x[bass.ds(b, 1), :, a * Q:(a + 1) * Q].rearrange("a (c r) i -> r (a c) i", r=SQ)
                                 ).then_inc(x_loaded, DMA)

            sp.dma_start(ids_row[:, :], ids.rearrange("(a b) -> a b", a=1)).then_inc(ids_loaded, DMA)
            load_x(0)
            load_W(0)
            load_W(1)
            load_mask(0, 0)
            sp.dma_start(coeffs[:, :], coeff_dram).then_inc(coeffs_loaded, DMA)
            load_W(2)
            load_W(3)
            load_mask(0, 1)
            with nc.allow_non_contiguous_dma(reason="4 KiB of bias, once"):
                sp.dma_start(bias_col[:, :].rearrange("p (h k) -> p h k", k=4), bias_dram).then_inc(bias_loaded, DMA)
            sp.wait_ge(ids_loaded, DMA)

            def slot(kind, b, u, par):
                on = stages(kind, u)
                if u == 0 and kind in ("first", "steady"):
                    sp.wait_ge(x_turn_done, 4 * (b + 1))
                    load_x(b + 1)
                if u % 4 == 3 and kind in ("first", "steady"):
                    sp.wait_ge(M_done, 8 * b + u + 1)
                    load_mask(b + 1, u // 4)
                t = u - 2 if kind == "lead" else u + 6
                if kind == "lead" or (kind == "first" and t < 8):
                    sp.wait_ge(tile_turned, t - 3)
                    load_W(t)
                elif (kind == "first" and u >= 5 - T_AHEAD) or kind in ("steady", "last") \
                        or (kind == "drain" and u < 5 - T_AHEAD):
                    m = (u + T_AHEAD + 3) % 8
                    bw = b - 1 + (u + T_AHEAD + 3) // 8
                    who = sp.value_load(ids_row[0:1, bass.ds(bw, 1)], min_val=0, max_val=weight.shape[0] - 1)
                    if kind == "first" and m < 4:
                        sp.wait_ge(tile_turned, m + 5)
                    else:
                        sp.wait_ge(dve_took, 8 * bw + m - 3)
                    if by_dve(m):
                        q, half = m // 2, m % 2
                        for a in range(GRP):
                            sp.dma_start(natural[a * SQ:(a + 1) * SQ, m % 4, :].rearrange("r (c f) -> r c f", f=P),
                                         weight[bass.ds(who, 1), q * Q:(q + 1) * Q,
                                                half * HALF + a * P:half * HALF + (a + 1) * P]
                                         .rearrange("a (c r) f -> r (a c) f", r=SQ)).then_inc(natural_loaded[m % 4], DMA)
                    else:
                        sp.dma_start(natural[:, m % 4, :],
                                     weight[bass.ds(who, 1), m * P:(m + 1) * P, :].rearrange("a p i -> (a p) i")
                                     ).then_inc(natural_loaded[m % 4], DMA)
                if on["second"]:
                    sp.wait_ge(out_taken, 8 * (b - 1) + u + 3)
                    s, q = u % ST, u // ST
                    sp.dma_start(out[bass.ds(b - 1, 1), s * P:(s + 1) * P, q * Q:(q + 1) * Q]
                                 .rearrange("a p c -> (a p) c"), out_sb[:, u % 2, :]).then_inc(stored[u % 2], DMA)

            batches(sp, slot)
            for i in range(2):
                sp.wait_ge(stored[i], DMA * (B * K // 2 + 1))

        @block.gpsimd
        def _(pool):
            nc.gpsimd.memset(ident[:, :], 0.0).then_inc(ident_steps, 1)
            pool.wait_ge(ident_steps, 1)
            nc.gpsimd.affine_select(out=ident[:, :], in_=ident[:, :], compare_op=ALU.not_equal, fill=1.0, base=0,
                                    pattern=[[-1, P]], channel_multiplier=1).then_inc(ident_steps, 1)
            pool.wait_ge(ident_steps, 2)
            for t in range(K):
                pool.wait_ge(natural_loaded[t % 4], DMA * (t // 4 + 1))
                nc.gpsimd.tensor_tensor(natural[:, t % 4, out_columns(t)], natural[:, t % 4, out_columns(t)],
                                        ident[:, :], ALU.add).then_inc(diag_added, 1)
            with pool.Fori(0, B) as b:
                for m in range(K):
                    if not adds_diagonal(m):
                        continue
                    pool.wait_ge(natural_loaded[m % 4], landed(b, m))
                    pool.wait_ge(diag_added, diagonals(b, m) - 1)
                    if by_dve(m):
                        for a in (2 * (m // 2 % 2), 2 * (m // 2 % 2) + 1):
                            at = slice(a * SQ, (a + 1) * SQ)
                            row = natural[at, m % 4, a % 2 * HALF:a % 2 * HALF + SQ]
                            one = ident[at, at]
                            diag = bass.AP(row.tensor, row.offset, [row.ap[0], (P + SQ, GRP), (1, SQ)])
                            ones = bass.AP(one.tensor, one.offset, [one.ap[0], (0, GRP), (1, SQ)])
                            done = nc.gpsimd.tensor_tensor(diag, diag, ones, ALU.add)
                            if a % 2 == 0:
                                done.then_inc(half_diag_added, 1)
                                pool.wait_ge(half_diag_added,
                                             up_to(lambda j: by_dve(j) and adds_diagonal(j), b, m))
                    else:
                        block_m = natural[:, m % 4, m * P:(m + 1) * P]
                        done = nc.gpsimd.tensor_tensor(block_m, block_m, ident[:, :], ALU.add)
                    done.then_inc(diag_added, 1)

        @block.tensor
        def _(pe):
            pe.wait_ge(ident_steps, 2)

            def turn(r, columns):
                for k in range(K):
                    done = nc.tensor.transpose(turn_ps[:, r % 2, k, :], columns(natural[:, r % 4, :], k), ident[:, :])
                done.then_inc(tile_turned, 1)

            def product(acc, terms):
                for k in range(K):
                    for j, (left, right) in enumerate(terms(k)):
                        done = nc.tensor.matmul(acc, left, right, start=(k == 0 and j == 0),
                                                stop=(k == K - 1 and j == 2))
                return done

            def slot(kind, b, u, par):
                on = stages(kind, u)

                def turn_W():
                    for t in on["turn_W"]:
                        pe.wait_ge(diag_added, t + 1)
                        if t >= 2:
                            pe.wait_ge(act_took, t - 1)
                        turn(t, lambda tile, k: tile[:, k:D:K])

                if kind == "lead":
                    turn_W()
                bw, m = b - 1 + (u + T_AHEAD) // 8, (u + T_AHEAD) % 8
                if on["turn_w"] and not by_dve(m):
                    pe.wait_ge(diag_added, diagonals(bw, m))
                    pe.wait_ge(act_took, 8 * bw + m + 1)
                    turn(m, lambda tile, k: tile[:, out_columns(k)])
                if on["first"]:
                    if u == 0:
                        pe.wait_ge(x_done, 4 * (b + 1))
                    pe.wait_ge(M_done, 8 * b + u + 1)
                    if kind != "first" or u >= 2:
                        pe.wait_ge(h_done, 8 * b + u - 1)
                    product(first_ps[:, u % 2, 0:S], lambda k: (
                        (M_hi[:, u % 2, k, :], x_lo[:, par, k, :]),
                        (M_hi[:, u % 2, k, :], x_hi[:, par, k, :]),
                        (M_lo[:, u % 2, k, :], x_hi[:, par, k, :]))).then_inc(first_done, 1)
                if kind == "first":
                    turn_W()
                if on["second"]:
                    s, q = u % ST, u // ST
                    if u == 0:
                        pe.wait_ge(h_done, 8 * b)
                    if s == 0:
                        pe.wait_ge(dve_took, 8 * (b - 1) + u + 2)
                    pe.wait_ge(out_taken, 8 * (b - 1) + u + 1)
                    rows = slice(s * P, (s + 1) * P)
                    product(second_ps[:, u % 2, 0:Q], lambda k: (
                        (h_hi[:, 1 - par, k, rows], w_lo[:, q % 2, k, :]),
                        (h_hi[:, 1 - par, k, rows], w_hi[:, q % 2, k, :]),
                        (h_lo[:, 1 - par, k, rows], w_hi[:, q % 2, k, :]))).then_inc(second_done, 1)

            batches(pe, slot)

        @block.scalar
        def _(act):
            act.sem_inc(out_taken, 2)
            for i in range(2):
                act.sem_inc(stored[i], DMA)
            def slot(kind, b, u, par):
                on = stages(kind, u)
                v = u + M_AHEAD

                def split_x():
                    for j in on["x_pairs"]:
                        act.wait_ge(x_turn_done, 4 * (b + 1) + j + 1)
                        nc.scalar.copy(x_hi[:, 1 - par, :, j * 2 * SQ:(j + 1) * 2 * SQ], x_turned[:, j % 2, :, :]
                                       ).then_inc(x_hi_done, 1)

                def copy_W():
                    for t in on["turn_W"]:
                        act.wait_ge(tile_turned, t + 1)
                        nc.scalar.copy(WT[:, :, t * P:(t + 1) * P], turn_ps[:, t % 2, :, :]).then_inc(act_took, 1)

                if kind == "lead":
                    split_x()
                if kind == "lead" and not on["split_M"]:
                    copy_W()
                if on["split_M"]:
                    act.wait_ge(sum_done, 8 * b + v + 1)
                    nc.scalar.copy(M_hi[:, v % 2, :, :], unit(v).bitcast(F32)).then_inc(M_hi_done, 1)
                if on["sum_M"]:
                    if (v + 1) % 4 == 0:
                        half = (v + 1) // 4
                        act.wait_ge(mask_loaded[half % 2], DMA * (b + half // 2 + 1))
                    nc.scalar.activation(unit(v + 1).bitcast(F32), unit(v + 1), ACT.Copy, scale=2.0, bias=-1.0
                                         ).then_inc(sign_done, 1)
                if kind == "lead" and on["split_M"]:
                    copy_W()
                if on["turn_w"]:
                    bw, m = b - 1 + (u + T_AHEAD) // 8, (u + T_AHEAD) % 8
                    q = m // 2
                    if by_dve(m):
                        act.wait_ge(unit_turned, turned(bw, m))
                        nc.scalar.copy(w_hi[:, q % 2, m % 2 * 4:m % 2 * 4 + 4, :],
                                       natural[:, m % 4, :].rearrange("p (c k) -> p k c", k=4)).then_inc(act_took, 1)
                    else:
                        act.wait_ge(tile_turned, turned(bw, m))
                        nc.scalar.copy(w_hi[:, q % 2, :, m % 2 * P:(m % 2 + 1) * P], turn_ps[:, m % 2, :, :]
                                       ).then_inc(act_took, 1)
                if kind != "lead":
                    split_x()
                if on["first"]:
                    if kind == "first" and u == 0:
                        act.wait_ge(bias_loaded, DMA)
                    act.wait_ge(first_done, 8 * b + u + 1)
                    nc.scalar.activation(h_hi[:, par, u, :], first_ps[:, u % 2, 0:S], ACT.Identity,
                                         bias=bias_col[:, u:u + 1], scale=1.0).then_inc(h_hi_done, 1)
                if kind == "first":
                    copy_W()
                if on["second"]:
                    act.wait_ge(second_done, 8 * (b - 1) + u + 1)
                    act.wait_ge(stored[u % 2], DMA * (4 * (b - 1) + u // 2 + 1))
                    nc.scalar.copy(out_sb[:, u % 2, :], second_ps[:, u % 2, 0:Q]).then_inc(out_taken, 1)

            batches(act, slot)

        @block.vector
        def _(dve):
            def split_h(b, u, par):
                dve.wait_ge(h_hi_done, 8 * b + u + 1)
                nc.vector.scalar_tensor_tensor(out=h_lo[:, par, u, :], in0=first_ps[:, u % 2, 0:S],
                                               scalar=bias_col[:, u:u + 1], in1=h_hi[:, par, u, :].bitcast(F32),
                                               op0=ALU.add, op1=ALU.subtract).then_inc(h_done, 1)

            def turn_x(b, j):
                dve.wait_ge(x_loaded, GRP * DMA * (b + 2))
                if b >= 0 or j >= 2:
                    dve.wait_ge(x_done, 4 * (b + 1) + j - 1)
                nc.vector.transpose(
                    x_turned[:, j % 2, :, :].rearrange("p k (c r) -> p c k r", c=2),
                    x_nat[:, 2 * j:2 * j + 2, :].rearrange("p c (i k) -> p c k i", k=K)).then_inc(x_turn_done, 1)

            def split_x(b, j, par):
                dve.wait_ge(x_hi_done, 4 * (b + 1) + j + 1)
                at = slice(j * 2 * SQ, (j + 1) * 2 * SQ)
                nc.vector.tensor_tensor(x_lo[:, 1 - par, :, at], x_turned[:, j % 2, :, :],
                                        x_hi[:, 1 - par, :, at].bitcast(F32), ALU.subtract).then_inc(x_done, 1)

            def slot(kind, b, u, par):
                on = stages(kind, u)
                v = u + M_AHEAD
                if kind == "lead" and on["x_pairs"]:
                    turn_x(b, 0)
                    for j in range(1, 4):
                        turn_x(b, j)
                        split_x(b, j - 1, par)
                    split_x(b, 3, par)
                    dve.wait_ge(coeffs_loaded, DMA)
                bw, m = b - 1 + (u + T_AHEAD) // 8, (u + T_AHEAD) % 8
                if on["turn_w"] and by_dve(m):
                    if adds_diagonal(m):
                        dve.wait_ge(diag_added, diagonals(bw, m))
                    else:
                        dve.wait_ge(natural_loaded[m % 4], landed(bw, m))
                    blocks = natural[:, m % 4, :].rearrange("p (c j k) -> p c k j", j=SQ, k=4)
                    nc.vector.transpose(blocks, blocks).then_inc(unit_turned, 1)
                if kind != "lead":
                    for j in on["x_pairs"]:
                        turn_x(b, j)
                if on["split_M"]:
                    dve.wait_ge(M_hi_done, 8 * b + v + 1)
                    nc.vector.tensor_tensor(M_lo[:, v % 2, :, :], unit(v).bitcast(F32),
                                            M_hi[:, v % 2, :, :].bitcast(F32), ALU.subtract).then_inc(M_done, 1)
                if on["sum_M"]:
                    if kind == "lead" or (kind == "first" and v < 7):
                        dve.wait_ge(act_took, 8 * b + v + 2)
                    dve.wait_ge(sign_done, 8 * b + v + 2)
                    o = (v + 1) % 8 * P
                    nc.vector.scalar_tensor_tensor(out=unit(v + 1).bitcast(F32), in0=unit(v + 1).bitcast(F32),
                                                   scalar=coeffs[:, bass.ds(b + (v + 1) // 8, 1)],
                                                   in1=WT[:, :, o:o + P], op0=ALU.mult, op1=ALU.add
                                                   ).then_inc(sum_done, 1)
                if on["turn_w"]:
                    q = m // 2
                    dve.wait_ge(act_took, K + 8 * bw + m + 1)
                    if by_dve(m):
                        at = (slice(None), q % 2, slice(m % 2 * 4, m % 2 * 4 + 4), slice(None))
                        turned = natural[:, m % 4, :].rearrange("p (c k) -> p k c", k=4)
                    else:
                        at = (slice(None), q % 2, slice(None), slice(m % 2 * P, (m % 2 + 1) * P))
                        turned = turn_ps[:, m % 2, :, :]
                    nc.vector.tensor_tensor(w_lo[at], turned, w_hi[at].bitcast(F32), ALU.subtract).then_inc(dve_took, 1)
                if kind != "lead":
                    for j in on["x_pairs"]:
                        split_x(b, j, par)
                if on["first"]:
                    split_h(b, u, par)

            batches(dve, slot)


_INS = ["x", "condB_coeff", "itok_B_3_7", "mask_Bx4096x4096_ik1", "L0_cond_W", "L0_cond_b", "L1_cond_weight"]
_OUTS = [((8, 256, 1024), "float32")]


def kernel(**inputs):
    import numpy as _np
    import concourse.bacc as _bacc
    from concourse import mybir as _mybir
    from concourse.bass_utils import run_bass_kernel_spmd as _run

    nc = _bacc.Bacc("TRN2", target_bir_lowering=False, num_devices=1)
    arrays, args = {}, []
    for name in _INS:
        a = _np.ascontiguousarray(inputs[name])
        arrays[f"in_{name}_dram"] = a
        args.append(nc.dram_tensor(f"in_{name}_dram", a.shape, _mybir.dt.from_np(a.dtype), kind="ExternalInput").ap())
    for i, (shape, dtype) in enumerate(_OUTS):
        dt = _mybir.dt.from_np(_np.dtype(dtype))
        args.append(nc.dram_tensor(f"out_{i}_dram", shape, dt, kind="ExternalOutput").ap())
    build(nc, *args)
    r = _run(nc, [arrays], core_ids=[0])
    got = tuple(r.results[0][f"out_{i}_dram"] for i in range(len(_OUTS)))
    return got[0]
```

```python
from contextlib import ExitStack

import concourse.bass as bass
from concourse import mybir

P = 128
SQ = 32

F32 = mybir.dt.float32
F32R = mybir.dt.float32r
I32 = mybir.dt.int32
ALU = mybir.AluOpType
ACT = mybir.ActivationFunctionType

M_AHEAD = 1
W_AHEAD = M_AHEAD + 2
T_AHEAD = 2
DVE_UNITS = {"first": (2, 3, 4, 5, 6), "middle": (0, 1, 2, 3, 4, 5, 6), "last": (0, 1, 2, 3, 4, 5, 6, 7)}
WARM_UPS = 24
DMA = 16
X_HALVES = {4: (0,), 6: (1,)}
X_HALVES_FIRST = {3: (0,), 5: (1,)}


def stages(kind, u):
    return {
        "turn_W": (0,) if kind == "lead" and u == 7 - M_AHEAD else (1, 2) if kind == "lead"
        else (3,) if kind == "first" and u == 0
        else (u + W_AHEAD,) if kind == "first" and u < 8 - W_AHEAD else (),
        "turn_w": (kind == "first" and u >= 8 - T_AHEAD) or kind in ("steady", "last")
        or (kind == "drain" and u < 8 - T_AHEAD),
        "split_M": (kind == "lead" and u >= 8 - M_AHEAD) or kind in ("first", "steady")
        or (kind == "last" and u < 8 - M_AHEAD),
        "sum_M": kind in ("lead", "first", "steady") or (kind == "last" and u < 8 - M_AHEAD - 1),
        "turn_x": (0, 1) if kind == "lead" and u == 7 - M_AHEAD
        else X_HALVES_FIRST.get(u, ()) if kind == "first" else X_HALVES.get(u, ()) if kind == "steady" else (),
        "first": kind in ("first", "steady", "last"),
        "second": kind in ("steady", "last", "drain"),
    }


def place(kind):
    return {"first": "first", "drain": "last"}.get(kind, "middle")


def by_dve(m, where):
    return m in DVE_UNITS[where]


def by_pe(m, where):
    return not by_dve(m, where)


def adds_diagonal(m, where):
    return m % 2 == m // 4


def up_to(what, b, m, where, of=range(8)):
    before = sum(what(j, "middle") for j in of) * b
    if where != "first":
        before += sum(what(j, "first") - what(j, "middle") for j in of)
    return before + sum(what(j, where) for j in of if j <= m)


def build(nc, x, coeff, ids, mask, W, bias, weight, out):
    B, S, D = x.shape
    K = D // P
    ST = S // P
    CH = S // SQ
    Q = D // 4
    GRP = P // SQ
    HALF = D // 2
    assert K == 8 and ST == 2 and CH == 8 and Q == 2 * P and B >= 4 and B % 2 == 0

    with ExitStack() as ctx:
        def sb(name, shape, dt):
            return ctx.enter_context(nc.sbuf_tensor(name, shape, dt))

        def sem(name):
            return ctx.enter_context(nc.semaphore(name))

        ident = sb("ident", [P, P], F32)
        WT = sb("WT", [P, K, D], F32)
        coeffs = sb("coeffs", [P, B], F32)
        bias_col = sb("bias_col", [P, K], F32)
        ids_row = sb("ids_row", [1, B], I32)
        natural = sb("natural", [P, 4, D], F32)
        masks = sb("masks", [P, 2, K, HALF], I32)
        M_hi = sb("M_hi", [P, 2, K, P], F32R)
        M_lo = sb("M_lo", [P, 2, K, P], F32R)
        w_hi = sb("w_hi", [P, 2, K, Q], F32R)
        w_lo = sb("w_lo", [P, 2, K, Q], F32R)
        x_nat = sb("x_nat", [P, CH, Q], F32)
        x_turned = sb("x_turned", [P, K, S // 2], F32)
        x_hi = sb("x_hi", [P, 2, K, S], F32R)
        x_lo = sb("x_lo", [P, 2, K, S], F32R)
        h_hi = sb("h_hi", [P, 2, K, S], F32R)
        h_lo = sb("h_lo", [P, 2, K, S], F32R)
        out_sb = sb("out_sb", [P, 2, Q], F32)
        turn_ps = ctx.enter_context(nc.psum_tensor("turn_ps", [P, 2, 512], F32))
        first_ps = ctx.enter_context(nc.psum_tensor("first_ps", [P, 4, 512], F32))
        second_ps = ctx.enter_context(nc.psum_tensor("second_ps", [P, 2, 512], F32))

        ids_loaded = sem("ids_loaded")
        coeffs_loaded = sem("coeffs_loaded")
        bias_loaded = sem("bias_loaded")
        ident_steps = sem("ident_steps")
        natural_loaded = [sem(f"natural_loaded{i}") for i in range(4)]
        mask_loaded = [sem(f"mask_loaded{i}") for i in range(2)]
        x_loaded = sem("x_loaded")
        diag_added = sem("diag_added")
        half_diag_added = sem("half_diag_added")
        tile_turned = sem("tile_turned")
        unit_turned = sem("unit_turned")
        act_took = sem("act_took")
        dve_took = sem("dve_took")
        mask_part_loaded = sem("mask_part_loaded")
        sign_part_done = sem("sign_part_done")
        sum_part_done = sem("sum_part_done")
        M_hi_part_done = sem("M_hi_part_done")
        sign_done = sem("sign_done")
        sum_done = sem("sum_done")
        M_hi_done = sem("M_hi_done")
        M_done = sem("M_done")
        x_turn_done = sem("x_turn_done")
        x_hi_done = sem("x_hi_done")
        x_done = sem("x_done")
        first_done = sem("first_done")
        bias_added = sem("bias_added")
        h_hi_done = sem("h_hi_done")
        h_done = sem("h_done")
        second_done = sem("second_done")
        out_taken = sem("out_taken")
        stored = [sem(f"stored{i}") for i in range(2)]

        bias_dram = bias.rearrange("(h p k) -> p h k", p=P, k=4)
        coeff_dram = coeff.rearrange("(a b) -> a b", a=1).to_broadcast([P, B])

        def unit(v):
            return masks[:, v // 4 % 2, :, v % 4:HALF:4]

        PARTS = (slice(0, K // 2), slice(K // 2, K))

        def out_columns(u):
            return slice(u // 4 * HALF + u % 4, (u // 4 + 1) * HALF, 4)

        def landed(b, m, where):
            return DMA * (2 + up_to(lambda j, at: GRP if by_dve(j, at) else 1, b, m, where, of=(m % 4, m % 4 + 4)))

        def diagonals(b, m, where):
            return K + up_to(adds_diagonal, b, m, where)

        def turning(r):
            return (turn_ps if r % 2 else second_ps)[:, :, :].rearrange("p n (j r) -> p (n j) r", r=P)

        def turned_unit(m, where):
            if by_dve(m, where):
                return natural[:, m % 4, :].rearrange("p (o k) -> p k o", k=4)
            return turning(m).rearrange("p (k t) r -> p k (t r)", t=2)

        def turned(b, m, where):
            return up_to(by_dve, b, m, where) if by_dve(m, where) else K + up_to(by_pe, b, m, where)

        block = ctx.enter_context(nc.Block())

        def batches(eng, slot):
            for u in range(K - M_AHEAD - 1, K):
                slot("lead", -1, u, 1)
            for u in range(K):
                slot("first", 0, u, 0)
            with eng.Fori(0, (B - 2) // 2) as i:
                for par in (1, 0):
                    b = 2 * i + (1 if par else 2)
                    for u in range(K):
                        slot("steady", b, u, par)
            for u in range(K):
                slot("last", B - 1, u, (B - 1) % 2)
            for u in range(K):
                slot("drain", B, u, B % 2)

        @block.sync
        def _(sp):
            def load_W(t):
                sp.dma_start(natural[:, t % 4, :], W[out_columns(t), :]).then_inc(natural_loaded[t % 4], DMA)

            def load_mask(b, half):
                sp.dma_start(masks[:, half, :, :],
                             mask[bass.ds(b, 1), :, half * HALF:(half + 1) * HALF]
                             .rearrange("a (p k) c -> p (a k) c", k=K)).then_inc(mask_loaded[half], DMA)

            def load_x(b):
                for a in range(GRP):
                    sp.dma_start(x_nat[a * SQ:(a + 1) * SQ, :, :],
                                 x[bass.ds(b, 1), :, a * Q:(a + 1) * Q].rearrange("a (c r) i -> r (a c) i", r=SQ)
                                 ).then_inc(x_loaded, DMA)

            def load_unit(bw, m, where):
                who = sp.value_load(ids_row[0:1, bass.ds(bw, 1)], min_val=0, max_val=weight.shape[0] - 1)
                if where == "first" and m < 4:
                    sp.wait_ge(tile_turned, m + 5)
                else:
                    sp.wait_ge(dve_took, 8 * bw + m - 3)
                q, half = m // 2, m % 2
                if by_dve(m, where):
                    for a in range(GRP):
                        sp.dma_start(natural[a * SQ:(a + 1) * SQ, m % 4, :].rearrange("r (c f) -> r c f", f=P),
                                     weight[bass.ds(who, 1), q * Q:(q + 1) * Q,
                                            half * HALF + a * P:half * HALF + (a + 1) * P]
                                     .rearrange("a (c r) f -> r (a c) f", r=SQ)).then_inc(natural_loaded[m % 4], DMA)
                else:
                    sp.dma_start(natural[:, m % 4, :].rearrange("p (t i) -> p t i", t=2),
                                 weight[bass.ds(who, 1), q * Q:(q + 1) * Q, half * HALF:(half + 1) * HALF]
                                 .rearrange("a (t p) i -> p (a t) i", p=P)).then_inc(natural_loaded[m % 4], DMA)

            sp.dma_start(ids_row[:, :], ids.rearrange("(a b) -> a b", a=1)).then_inc(ids_loaded, DMA)
            load_x(0)
            load_W(0)
            for part, landed_here in ((0, mask_part_loaded), (1, mask_loaded[0])):
                sp.dma_start(masks[:, 0, part * K // 2:(part + 1) * K // 2, :],
                             mask[0:1, :, 0:HALF].rearrange("a (p k) c -> p (a k) c", k=K)
                             [:, part * K // 2:(part + 1) * K // 2, :]).then_inc(landed_here, DMA)
            sp.dma_start(coeffs[:, :], coeff_dram).then_inc(coeffs_loaded, DMA)
            load_W(1)
            load_W(2)
            load_W(3)
            with nc.allow_non_contiguous_dma(reason="4 KiB of bias, once"):
                sp.dma_start(bias_col[:, :].rearrange("p (h k) -> p h k", k=4), bias_dram).then_inc(bias_loaded, DMA)
            sp.wait_ge(ids_loaded, DMA)

            def slot(kind, b, u, par):
                on, where = stages(kind, u), place(kind)
                if u == 0 and kind in ("first", "steady"):
                    sp.wait_ge(x_turn_done, 2 * (b + 1))
                    load_x(b + 1)
                if u % 4 == 3 and kind in ("first", "steady"):
                    sp.wait_ge(M_done, 8 * b + u + 1)
                    load_mask(b + 1, u // 4)
                t = u - 2 if kind == "lead" else u + 6
                if kind == "lead" or (kind == "first" and t < 8):
                    sp.wait_ge(tile_turned, t - 3)
                    load_W(t)
                    if t == 5:
                        load_mask(0, 1)
                elif (kind == "first" and u >= 5 - T_AHEAD) or kind in ("steady", "last"):
                    load_unit(b - 1 + (u + T_AHEAD + 3) // 8, (u + T_AHEAD + 3) % 8, where)
                if (kind == "last" and u == 7) or (kind == "drain" and u < 4 - T_AHEAD):
                    load_unit(B - 1, (u + T_AHEAD + 4) % 8, "last")
                if on["second"]:
                    sp.wait_ge(out_taken, 8 * (b - 1) + u + 3)
                    s, q = u % ST, u // ST
                    sp.dma_start(out[bass.ds(b - 1, 1), s * P:(s + 1) * P, q * Q:(q + 1) * Q]
                                 .rearrange("a p c -> (a p) c"), out_sb[:, u % 2, :]).then_inc(stored[u % 2], DMA)

            batches(sp, slot)
            for i in range(2):
                sp.wait_ge(stored[i], DMA * (B * K // 2 + 1))

        @block.gpsimd
        def _(pool):
            nc.gpsimd.memset(ident[:, :], 0.0).then_inc(ident_steps, 1)
            pool.wait_ge(ident_steps, 1)
            nc.gpsimd.affine_select(out=ident[:, :], in_=ident[:, :], compare_op=ALU.not_equal, fill=1.0, base=0,
                                    pattern=[[-1, P]], channel_multiplier=1).then_inc(ident_steps, 1)
            pool.wait_ge(ident_steps, 2)
            for t in range(K):
                pool.wait_ge(natural_loaded[t % 4], DMA * (t // 4 + 1))
                nc.gpsimd.tensor_tensor(natural[:, t % 4, out_columns(t)], natural[:, t % 4, out_columns(t)],
                                        ident[:, :], ALU.add).then_inc(diag_added, 1)

            def add_diagonals(b, where):
                for m in range(K):
                    if not adds_diagonal(m, where):
                        continue
                    pool.wait_ge(natural_loaded[m % 4], landed(b, m, where))
                    pool.wait_ge(diag_added, diagonals(b, m, where) - 1)
                    if by_dve(m, where):
                        for a in (2 * (m // 2 % 2), 2 * (m // 2 % 2) + 1):
                            at = slice(a * SQ, (a + 1) * SQ)
                            row = natural[at, m % 4, a % 2 * HALF:a % 2 * HALF + SQ]
                            one = ident[at, at]
                            diag = bass.AP(row.tensor, row.offset, [row.ap[0], (P + SQ, GRP), (1, SQ)])
                            ones = bass.AP(one.tensor, one.offset, [one.ap[0], (0, GRP), (1, SQ)])
                            done = nc.gpsimd.tensor_tensor(diag, diag, ones, ALU.add)
                            if a % 2 == 0:
                                done.then_inc(half_diag_added, 1)
                                pool.wait_ge(half_diag_added,
                                             up_to(lambda j, at: by_dve(j, at) and adds_diagonal(j, at), b, m, where))
                    else:
                        row = natural[:, m % 4, m // 2 % 2 * Q:m // 2 % 2 * Q + P]
                        one = ident[:, :]
                        diag = bass.AP(row.tensor, row.offset, [row.ap[0], (HALF + P, 2), (1, P)])
                        ones = bass.AP(one.tensor, one.offset, [one.ap[0], (0, 2), (1, P)])
                        done = nc.gpsimd.tensor_tensor(diag, diag, ones, ALU.add)
                    done.then_inc(diag_added, 1)

            add_diagonals(0, "first")
            with pool.Fori(1, B - 1) as b:
                add_diagonals(b, "middle")
            add_diagonals(B - 1, "last")

        @block.tensor
        def _(pe):
            pe.wait_ge(ident_steps, 2)

            def turn(r, columns):
                for j in range(K):
                    done = nc.tensor.transpose(turning(r)[:, j, :], columns(natural[:, r % 4, :], j), ident[:, :])
                done.then_inc(tile_turned, 1)

            def product(acc, terms, before_last=None):
                for k in range(K):
                    if before_last and k == K - 2:
                        pe.wait_ge(*before_last)
                    for j, (left, right) in enumerate(terms(k)):
                        done = nc.tensor.matmul(acc, left, right, start=(k == 0 and j == 0),
                                                stop=(k == K - 1 and j == 2))
                return done

            def slot(kind, b, u, par):
                on, where = stages(kind, u), place(kind)

                def turn_W():
                    for t in on["turn_W"]:
                        pe.wait_ge(diag_added, t + 1)
                        if t >= 2:
                            pe.wait_ge(act_took, t - 1)
                        turn(t, lambda tile, k: tile[:, k:D:K])

                if kind == "lead":
                    if u == 7:
                        for _ in range(WARM_UPS):
                            nc.tensor.transpose(first_ps[:, 3, 0:P], ident[:, :], ident[:, :])
                    turn_W()
                bw, m = b - 1 + (u + T_AHEAD) // 8, (u + T_AHEAD) % 8
                if on["turn_w"] and by_pe(m, where):
                    if adds_diagonal(m, where):
                        pe.wait_ge(diag_added, diagonals(bw, m, where))
                    else:
                        pe.wait_ge(natural_loaded[m % 4], landed(bw, m, where))
                    pe.wait_ge(act_took, m + 7 if kind == "first" else 8 * bw + m + 1)
                    turn(m, lambda unit, j: unit[:, j % 2 * HALF + j // 2:(j % 2 + 1) * HALF:4])
                if on["first"]:
                    if u == 0:
                        pe.wait_ge(x_done, 2 * (b + 1))
                    pe.wait_ge(M_done, 8 * b + u + 1)
                    if kind != "first" or u >= 4:
                        pe.wait_ge(h_done, 8 * b + u - 3)
                    product(first_ps[:, u % 4, 0:S], lambda k: (
                        (M_hi[:, u % 2, k, :], x_lo[:, par, k, :]),
                        (M_hi[:, u % 2, k, :], x_hi[:, par, k, :]),
                        (M_lo[:, u % 2, k, :], x_hi[:, par, k, :]))).then_inc(first_done, 1)
                if kind == "first":
                    turn_W()
                if on["second"]:
                    s, q = u % ST, u // ST
                    if u == 0:
                        pe.wait_ge(h_done, 8 * b - 2)
                    if s == 0:
                        pe.wait_ge(dve_took, 8 * (b - 1) + u + 2)
                    pe.wait_ge(out_taken, 8 * (b - 1) + u + 1)
                    rows = slice(s * P, (s + 1) * P)
                    product(second_ps[:, u % 2, 0:Q], lambda k: (
                        (h_hi[:, 1 - par, k, rows], w_lo[:, q % 2, k, :]),
                        (h_hi[:, 1 - par, k, rows], w_hi[:, q % 2, k, :]),
                        (h_lo[:, 1 - par, k, rows], w_hi[:, q % 2, k, :])),
                        before_last=(h_done, 8 * b) if u == 0 else None
                    ).then_inc(second_done, 1)

            batches(pe, slot)

        @block.scalar
        def _(act):
            act.sem_inc(out_taken, 2)
            for i in range(2):
                act.sem_inc(stored[i], DMA)

            def slot(kind, b, u, par):
                on, where = stages(kind, u), place(kind)
                v = u + M_AHEAD

                def split_x():
                    for j in on["turn_x"]:
                        act.wait_ge(x_turn_done, 2 * (b + 1) + j + 1)
                        nc.scalar.copy(x_hi[:, 1 - par, :, j * S // 2:(j + 1) * S // 2], x_turned[:, :, :]
                                       ).then_inc(x_hi_done, 1)

                def copy_W():
                    for t in on["turn_W"]:
                        act.wait_ge(tile_turned, t + 1)
                        nc.scalar.copy(WT[:, :, t * P:(t + 1) * P], turning(t)).then_inc(act_took, 1)

                if kind == "lead":
                    split_x()
                if kind == "lead" and not on["split_M"]:
                    copy_W()
                if on["split_M"] and kind == "lead":
                    for part, formed, done in ((PARTS[0], sum_part_done, M_hi_part_done),
                                               (PARTS[1], sum_done, M_hi_done)):
                        act.wait_ge(formed, 1)
                        nc.scalar.copy(M_hi[:, 0, part, :], unit(0)[:, part, :].bitcast(F32)).then_inc(done, 1)
                elif on["split_M"]:
                    act.wait_ge(sum_done, 8 * b + v + 1)
                    nc.scalar.copy(M_hi[:, v % 2, :, :], unit(v).bitcast(F32)).then_inc(M_hi_done, 1)
                if on["sum_M"] and kind == "lead" and v == 7:
                    for part, loaded, done in ((PARTS[0], mask_part_loaded, sign_part_done),
                                               (PARTS[1], mask_loaded[0], sign_done)):
                        act.wait_ge(loaded, DMA)
                        nc.scalar.activation(unit(0)[:, part, :].bitcast(F32), unit(0)[:, part, :], ACT.Copy,
                                             scale=2.0, bias=-1.0).then_inc(done, 1)
                elif on["sum_M"]:
                    if (v + 1) % 4 == 0:
                        half = (v + 1) // 4
                        act.wait_ge(mask_loaded[half % 2], DMA * (b + half // 2 + 1))
                    nc.scalar.activation(unit(v + 1).bitcast(F32), unit(v + 1), ACT.Copy, scale=2.0, bias=-1.0
                                         ).then_inc(sign_done, 1)
                if kind == "lead" and on["split_M"]:
                    copy_W()
                if on["turn_w"]:
                    bw, m = b - 1 + (u + T_AHEAD) // 8, (u + T_AHEAD) % 8
                    q, half = m // 2, slice(m % 2 * 4, m % 2 * 4 + 4)
                    if by_dve(m, where):
                        act.wait_ge(unit_turned, turned(bw, m, where))
                    else:
                        act.wait_ge(tile_turned, turned(bw, m, where))
                    nc.scalar.copy(w_hi[:, q % 2, half, :], turned_unit(m, where)).then_inc(act_took, 1)
                if kind != "lead":
                    split_x()
                if on["first"]:
                    if kind == "first" and u == 0:
                        act.wait_ge(bias_loaded, DMA)
                    act.wait_ge(first_done, 8 * b + u + 1)
                    tile = first_ps[:, u % 4, 0:S]
                    nc.scalar.activation(tile, tile, ACT.Identity, bias=bias_col[:, u:u + 1], scale=1.0
                                         ).then_inc(bias_added, 1)
                    if u % 2:
                        act.wait_ge(bias_added, 8 * b + u + 1)
                        nc.scalar.copy(h_hi[:, par, u - 1:u + 1, :], first_ps[:, u % 4 - 1:u % 4 + 1, 0:S]
                                       ).then_inc(h_hi_done, 2)
                if kind == "first":
                    copy_W()
                if on["second"]:
                    act.wait_ge(second_done, 8 * (b - 1) + u + 1)
                    act.wait_ge(stored[u % 2], DMA * (4 * (b - 1) + u // 2 + 1))
                    nc.scalar.copy(out_sb[:, u % 2, :], second_ps[:, u % 2, 0:Q]).then_inc(out_taken, 1)

            batches(act, slot)

        @block.vector
        def _(dve):
            def split_h(b, u, par):
                dve.wait_ge(h_hi_done, 8 * b + u + 1)
                nc.vector.tensor_tensor(h_lo[:, par, u - 1:u + 1, :], first_ps[:, u % 4 - 1:u % 4 + 1, 0:S],
                                        h_hi[:, par, u - 1:u + 1, :].bitcast(F32), ALU.subtract).then_inc(h_done, 2)

            def turn_x(b, j):
                dve.wait_ge(x_loaded, GRP * DMA * (b + 2))
                if b >= 0 or j >= 1:
                    dve.wait_ge(x_done, 2 * (b + 1) + j)
                nc.vector.transpose(
                    x_turned[:, :, :].rearrange("p k (c r) -> p c k r", r=SQ),
                    x_nat[:, j * CH // 2:(j + 1) * CH // 2, :].rearrange("p c (i k) -> p c k i", k=K)
                ).then_inc(x_turn_done, 1)

            def split_x(b, j, par):
                dve.wait_ge(x_hi_done, 2 * (b + 1) + j + 1)
                at = slice(j * S // 2, (j + 1) * S // 2)
                nc.vector.tensor_tensor(x_lo[:, 1 - par, :, at], x_turned[:, :, :],
                                        x_hi[:, 1 - par, :, at].bitcast(F32), ALU.subtract).then_inc(x_done, 1)

            def turn_unit(bw, m, where):
                if adds_diagonal(m, where):
                    dve.wait_ge(diag_added, diagonals(bw, m, where))
                else:
                    dve.wait_ge(natural_loaded[m % 4], landed(bw, m, where))
                blocks = natural[:, m % 4, :].rearrange("p (c j k) -> p c k j", j=SQ, k=4)
                nc.vector.transpose(blocks, blocks).then_inc(unit_turned, 1)

            def slot(kind, b, u, par):
                on, where = stages(kind, u), place(kind)
                v = u + M_AHEAD
                if kind == "lead" and on["turn_x"]:
                    for j in on["turn_x"]:
                        turn_x(b, j)
                        split_x(b, j, par)
                    dve.wait_ge(coeffs_loaded, DMA)
                bw, m = b - 1 + (u + T_AHEAD) // 8, (u + T_AHEAD) % 8
                if on["turn_w"]:
                    for t in (m,) if kind != "drain" else (m, m + 1) if u == 0 else (m + 1,) if m < 7 else ():
                        if by_dve(t, where):
                            turn_unit(bw, t, where)
                if kind != "lead":
                    for j in on["turn_x"]:
                        turn_x(b, j)
                if on["split_M"] and kind == "lead":
                    dve.wait_ge(M_hi_part_done, 1)
                    nc.vector.tensor_tensor(M_lo[:, 0, PARTS[0], :], unit(0)[:, PARTS[0], :].bitcast(F32),
                                            M_hi[:, 0, PARTS[0], :].bitcast(F32), ALU.subtract)
                    dve.wait_ge(M_hi_done, 1)
                    nc.vector.tensor_tensor(M_lo[:, 0, PARTS[1], :], unit(0)[:, PARTS[1], :].bitcast(F32),
                                            M_hi[:, 0, PARTS[1], :].bitcast(F32), ALU.subtract).then_inc(M_done, 1)
                elif on["split_M"]:
                    dve.wait_ge(M_hi_done, 8 * b + v + 1)
                    nc.vector.tensor_tensor(M_lo[:, v % 2, :, :], unit(v).bitcast(F32),
                                            M_hi[:, v % 2, :, :].bitcast(F32), ALU.subtract).then_inc(M_done, 1)
                if on["sum_M"] and kind == "lead" and v == 7:
                    dve.wait_ge(act_took, 1)
                    for part, formed, done in ((PARTS[0], sign_part_done, sum_part_done),
                                               (PARTS[1], sign_done, sum_done)):
                        dve.wait_ge(formed, 1)
                        nc.vector.scalar_tensor_tensor(out=unit(0)[:, part, :].bitcast(F32),
                                                       in0=unit(0)[:, part, :].bitcast(F32), scalar=coeffs[:, 0:1],
                                                       in1=WT[:, part, 0:P], op0=ALU.mult, op1=ALU.add
                                                       ).then_inc(done, 1)
                elif on["sum_M"]:
                    if kind == "lead" or (kind == "first" and v < 7):
                        dve.wait_ge(act_took, 8 * b + v + 2)
                    dve.wait_ge(sign_done, 8 * b + v + 2)
                    o = (v + 1) % 8 * P
                    nc.vector.scalar_tensor_tensor(out=unit(v + 1).bitcast(F32), in0=unit(v + 1).bitcast(F32),
                                                   scalar=coeffs[:, bass.ds(b + (v + 1) // 8, 1)],
                                                   in1=WT[:, :, o:o + P], op0=ALU.mult, op1=ALU.add
                                                   ).then_inc(sum_done, 1)
                if on["turn_w"]:
                    q = m // 2
                    dve.wait_ge(act_took, K + 8 * bw + m + 1)
                    at = (slice(None), q % 2, slice(m % 2 * 4, m % 2 * 4 + 4), slice(None))
                    nc.vector.tensor_tensor(w_lo[at], turned_unit(m, where), w_hi[at].bitcast(F32), ALU.subtract
                                            ).then_inc(dve_took, 1)
                if kind != "lead":
                    for j in on["turn_x"]:
                        split_x(b, j, par)
                if on["first"] and u % 2:
                    split_h(b, u, par)

            batches(dve, slot)


_INS = ["x", "condB_coeff", "itok_B_3_7", "mask_Bx4096x4096_ik1", "L0_cond_W", "L0_cond_b", "L1_cond_weight"]
_OUTS = [((8, 256, 1024), "float32")]


def kernel(**inputs):
    import numpy as _np
    import concourse.bacc as _bacc
    from concourse import mybir as _mybir
    from concourse.bass_utils import run_bass_kernel_spmd as _run

    nc = _bacc.Bacc("TRN2", target_bir_lowering=False, num_devices=1)
    arrays, args = {}, []
    for name in _INS:
        a = _np.ascontiguousarray(inputs[name])
        arrays[f"in_{name}_dram"] = a
        args.append(nc.dram_tensor(f"in_{name}_dram", a.shape, _mybir.dt.from_np(a.dtype), kind="ExternalInput").ap())
    for i, (shape, dtype) in enumerate(_OUTS):
        dt = _mybir.dt.from_np(_np.dtype(dtype))
        args.append(nc.dram_tensor(f"out_{i}_dram", shape, dt, kind="ExternalOutput").ap())
    build(nc, *args)
    r = _run(nc, [arrays], core_ids=[0])
    got = tuple(r.results[0][f"out_{i}_dram"] for i in range(len(_OUTS)))
    return got[0]
```
